# Optimizing a Trainium2 kernel written in Bass

```python
import numpy as np
import jax
import jax.numpy as jnp

def _softmax(x, axis=-1):
    return jax.nn.softmax(x, axis=axis)

def _gelu(x):
    return jax.nn.gelu(x, approximate=True)

def _silu(x):
    return jax.nn.silu(x)

def _sigmoid(x):
    return jax.nn.sigmoid(x)

def _layernorm(x, axis=-1, eps=1e-05):
    m = jnp.mean(x, axis=axis, keepdims=True)
    v = jnp.var(x, axis=axis, keepdims=True)
    return (x - m) / jnp.sqrt(v + eps)

def _scatter_add(tgt, idx, src, axis=0):
    return tgt.at[idx].add(src)

def _segment_sum(src, seg, n):
    return jax.ops.segment_sum(src, seg, n)
kernel_name = 'mk_adj_preln_d1_adj_r2_28c775'

def setup_inputs(seed: int=0):
    np.random.seed(seed)
    _w = jnp.asarray

    def _rec_inputs():
        import jax
        import jax.numpy as jnp
        _gk = jax.random.key(seed)
        x = -0.000929 + 1 * jax.random.normal(jax.random.fold_in(_gk, 1), (8192, 128), jnp.float32)
        _a = jax.random.bernoulli(jax.random.fold_in(_gk, 2), 0.000976562, (8192, 8192))
        _af = _a.astype(jnp.float32)
        adj = _af
        return (x, adj)
    x, adj = _rec_inputs()

    def _L0_gnn_setup():
        import jax, jax.numpy as jnp
        import numpy as np
        N, D = (4096, 128)
        EDGE_PROB = 0.005
        COS_EPS = 1e-08
        key = jax.random.key(seed)
        kx, ka = jax.random.split(key)
        x = jax.random.normal(kx, (N, D), dtype=jnp.float32)
        adj = (jax.random.uniform(ka, (N, N)) < EDGE_PROB).astype(jnp.float32)
        return {'t': jnp.float32(0.0), 'x': x, 'adj': adj, 'alpha': jnp.float32(0.5), 'beta': jnp.float32(1.0)}
    _L0_gnn_all = _L0_gnn_setup()
    _L0_gnn_in = {k: v for k, v in _L0_gnn_all.items() if k in ('t', 'alpha', 'beta')}
    del _L0_gnn_all
    return {'x': x, 'adj': adj, 'L0_gnn_t': _L0_gnn_in['t'], 'L0_gnn_alpha': _L0_gnn_in['alpha'], 'L0_gnn_beta': _L0_gnn_in['beta']}

def reference(x, adj, L0_gnn_t, L0_gnn_alpha, L0_gnn_beta):
    import jax
    import jax.numpy as jnp

    def _L0_gnn_ref(t, x, adj, alpha, beta):
        import jax, jax.numpy as jnp
        import numpy as np
        N, D = (4096, 128)
        EDGE_PROB = 0.005
        COS_EPS = 1e-08
        deg = jnp.clip(adj.sum(axis=1), 1.0)
        dis = deg ** (-0.5)
        adj_norm = dis[:, None] * adj * dis[None, :]
        diffusion = adj_norm @ x - x
        norms = jnp.maximum(jnp.linalg.norm(x, axis=-1), COS_EPS)
        sim = x @ x.T / (norms[:, None] * norms[None, :])
        attn = jax.nn.softmax(beta * sim * adj, axis=1)
        attn = jax.lax.stop_gradient(attn)
        return diffusion + jax.nn.sigmoid(alpha) * (attn @ x - x)
    h = jnp.maximum(_layernorm(x, axis=-1), 0.0)
    x = x + _L0_gnn_ref(L0_gnn_t, h, adj, L0_gnn_alpha, L0_gnn_beta)
    return x

_drawn_inputs = setup_inputs


def setup_inputs(seed=0):
    import zlib

    import numpy as np

    out = dict(_drawn_inputs(seed))
    spreads = {}
    factors = {}
    for name, (base, spread) in spreads.items():
        noise = np.random.default_rng([zlib.crc32(name.encode()), seed]).standard_normal(out[name].shape)
        drawn = base * np.exp(spread * noise) if base else spread * noise
        out[name] = jnp.asarray(drawn.astype(out[name].dtype))
    for name, factor in factors.items():
        out[name] = (out[name] * factor).astype(out[name].dtype)
    return out
```

```python
import numpy as np

import concourse.bass as bass
from concourse import mybir

P = 128
LN_EPS = 1e-5
COS_EPS = 1e-8


def gnn_block_kernel(nc, x, adj, alpha, beta, out):
    fp32 = mybir.dt.float32
    fp32r = mybir.dt.float32r
    fp16 = mybir.dt.float16
    bf16 = mybir.dt.bfloat16
    ALU = mybir.AluOpType
    ACT = mybir.ActivationFunctionType

    N = x.shape[0]
    TILES = N // P
    PT = 8
    PW = PT * P
    PANELS = N // PW
    HALF = 512
    LOAD = 4
    BODY = 8
    BODIES = TILES // BODY
    UNITS = PANELS * TILES
    GROUPS = TILES // PT

    x_t = x.rearrange("(t p) d -> p t d", p=P)
    out_t = out.rearrange("(t p) d -> p t d", p=P)
    adj_t = adj.rearrange("(t p) j -> p t j", p=P)
    adjT_dram = nc.dram_tensor("adjT_scratch", [UNITS // LOAD, P, LOAD * PW], bf16).ap()
    adjT_chunks = adjT_dram.rearrange("c p n -> p c n")

    from contextlib import ExitStack
    ctx = ExitStack()
    with ctx:
        def sb(name, shape, dt):
            return ctx.enter_context(nc.sbuf_tensor(name, shape, dt))

        def ps(name, shape, dt):
            return ctx.enter_context(nc.psum_tensor(name, shape, dt))

        def sem(name):
            return ctx.enter_context(nc.semaphore(name))

        h = sb("h", [P, TILES, P], fp32)
        uT_hi = sb("uT_hi", [P, N], fp16)
        uT_lo = sb("uT_lo", [P, N], fp16)
        adj_in = sb("adj_in", [P, 2, PT, LOAD * P], fp32)
        adjT = sb("adjT", [P, 2, LOAD, PW], bf16)
        ework = sb("ework", [P, 4, PW], fp32)
        e_hi = sb("e_hi", [P, 2, PW], fp32r)
        e_lo = sb("e_lo", [P, 2, PW], fp32r)
        hs_hi = sb("hs_hi", [P, 2, P], fp32r)
        hs_lo = sb("hs_lo", [P, 2, P], fp32r)
        esum = sb("esum", [P, PW], fp32)
        attnT = sb("attnT", [P, N], fp32)
        ident32 = sb("ident32", [P, P], fp32)
        ident16 = sb("ident16", [P, P], fp16)
        identb = sb("identb", [P, P], bf16)
        ones32 = sb("ones32", [P, P], fp32)
        onesb = sb("onesb", [P, 1], bf16)
        ab_row = sb("ab_row", [1, 2], fp32)
        ab = sb("ab", [P, 2], fp32)
        neg_half_beta = sb("neg_half_beta", [P, 1], fp32)
        gate = sb("gate", [P, 1], fp32)
        gate_tmp = sb("gate_tmp", [P, 2], fp32)
        neg_1_gate = sb("neg_1_gate", [P, 1], fp32)
        deg = sb("deg", [P, TILES], fp32)
        zsum = sb("zsum", [P, TILES], fp32)
        dis = sb("dis", [P, TILES], fp32)
        gz = sb("gz", [P, TILES], fp32)
        stats = sb("stats", [P, TILES, 6], fp32)
        mv = sb("mv", [P, TILES, 2], fp32)
        va = sb("va", [P, TILES], fp32)
        vb = sb("vb", [P, TILES], fp32)
        vc = sb("vc", [P, TILES], fp32)
        rstd = sb("rstd", [P, TILES], fp32)
        shift = sb("shift", [P, TILES], fp32)
        ssq = sb("ssq", [P, TILES], fp32)
        rnorm = sb("rnorm", [P, TILES], fp32)

        cos_ps = ps("cos_ps", [P, 2, PW], fp32)
        attn_ps = ps("attn_ps", [P, PW], fp32)
        adjT_ps = ps("adjT_ps", [P, PW], bf16)
        sums_ps = ps("sums_ps", [P, HALF], fp32)
        deg_ps = sums_ps[:, 0:PT]
        z_ps = sums_ps[:, PT:2 * PT]
        ab_ps = sums_ps[:, 2 * PT:2 * PT + 2]

        rows16 = [tuple(adjT[:, 1, 2 * parity + part, :].bitcast(fp16) for part in range(2)) for parity in range(2)]
        adj_bf = adj_in[:, :, :, :].bitcast(bf16).rearrange("p s t (c two) -> p s t c two", two=2)
        uT_ps = [cos_ps[:, 0, 0:HALF].bitcast(fp16), cos_ps[:, 0, HALF:PW].bitcast(fp16)]
        LSLOTS = 4
        adjT_in = adj_in[:, :, :, :].bitcast(bf16).rearrange(
            "p s t c -> p (s t c)").rearrange("p (s k i) -> p s k i", s=LSLOTS, k=LOAD)
        dh_hi, dh_lo = uT_hi, uT_lo

        consts_ready = sem("consts_ready")
        idents_ready = sem("idents_ready")
        ab_loaded = sem("ab_loaded")
        ab_bcast = sem("ab_bcast")
        ab_copied = sem("ab_copied")
        alpha_exp = sem("alpha_exp")
        scalars_ready = sem("scalars_ready")
        x_loaded = [sem(f"x_loaded{g}") for g in range(2)]
        vec_chain = sem("vec_chain")
        var_ready = sem("var_ready")
        std_ready = sem("std_ready")
        ln_ready = sem("ln_ready")
        h_ready = sem("h_ready")
        ssq_ready = sem("ssq_ready")
        norm_root = sem("norm_root")
        rnorm_ready = sem("rnorm_ready")
        u_ready = sem("u_ready")
        u_split = sem("u_split")
        uT_done = sem("uT_done")
        uT_copied = sem("uT_copied")

        adj_loaded = [sem(f"adj_loaded{s}") for s in range(2)]
        adjT_stored = [sem(f"adjT_stored{s}") for s in range(2)]
        transposed = sem("transposed")
        adjT_ready = sem("adjT_ready")
        cos_done = sem("cos_done")
        x_done = sem("x_done")
        ehi_done = sem("ehi_done")
        e_done = sem("e_done")
        hshi_done = sem("hshi_done")
        hslo_done = sem("hslo_done")
        elo_done = sem("elo_done")
        esum_done = sem("esum_done")
        attn_done = sem("attn_done")
        attn_copied = sem("attn_copied")
        deg_copied = sem("deg_copied")
        z_done = sem("z_done")
        z_copied = sem("z_copied")

        deg_ready = sem("deg_ready")
        deg_root = sem("deg_root")
        dis_ready = sem("dis_ready")
        dh_scaled = sem("dh_scaled")
        dh_ready = sem("dh_ready")
        adjT_loaded = [sem(f"adjT_loaded{s}") for s in range(LSLOTS)]
        diff_used = sem("diff_used")
        diffT_copied = sem("diffT_copied")
        back_done = sem("back_done")
        back_used = sem("back_used")
        x_again = [sem(f"x_again{s}") for s in range(2)]
        base_ready = sem("base_ready")
        out_ready = sem("out_ready")
        out_stored = [sem(f"out_stored{s}") for s in range(2)]

        block = ctx.enter_context(nc.Block())

        def is_first(b):
            return isinstance(b, int) and b == 0

        @block.sync
        def _(sp):
            sp.dma_start(ab_row[0:1, 0:1], alpha).then_inc(ab_loaded, 16)
            sp.dma_start(ab_row[0:1, 1:2], beta).then_inc(ab_loaded, 16)
            for g in range(2):
                T2 = TILES // 2
                sp.dma_start(h[:, g * T2:(g + 1) * T2, :], x_t[:, g * T2:(g + 1) * T2, :]).then_inc(x_loaded[g], 16)

            def body(panel, b, b_in_panel, last=False):
                for s in range(2):
                    if not is_first(b):
                        sp.wait_ge(transposed, b * BODY + (s - 1) * LOAD)
                    sp.dma_start(adj_in[:, s, :, :],
                                 adj_t[:, bass.ds(panel * PT, PT), bass.ds((b_in_panel * 2 + s) * LOAD * P, LOAD * P)]
                                 ).then_inc(adj_loaded[s], 16)
                    if not is_first(b):
                        store(b - 1, s)

            def store(b, s):
                sp.wait_ge(adjT_ready, b * BODY + (s + 1) * LOAD)
                sp.dma_start(adjT_chunks[:, bass.ds(b * 2 + s, 1), :],
                             adjT[:, s, :, :].rearrange("p (o k) i -> p o (k i)", o=1)).then_inc(adjT_stored[s], 16)

            body(0, 0, 0)
            with sp.Fori(1, BODIES) as c:
                body(0, c, c)
            with sp.Fori(1, PANELS) as panel:
                with sp.Fori(0, BODIES) as c:
                    body(panel, panel * BODIES + c, c)
            for s in range(2):
                store(PANELS * BODIES - 1, s)

            CHUNKS = UNITS // LOAD
            for s in range(2):
                sp.wait_ge(adjT_stored[s], 16 * PANELS * BODIES)
            sp.wait_ge(transposed, UNITS)
            for s in range(LSLOTS):
                sp.dma_start(adjT_in[:, s, :, :].rearrange("p k i -> p (k i)"),
                             adjT_dram[s, :, :]).then_inc(adjT_loaded[s], 16)
            with sp.Fori(1, CHUNKS // LSLOTS) as r:
                for s in range(LSLOTS):
                    sp.wait_ge(diff_used, (r - 1) * LSLOTS + s + 1)
                    sp.dma_start(adjT_in[:, s, :, :].rearrange("p (o k) i -> p o (k i)", o=1),
                                 adjT_chunks[:, bass.ds(r * LSLOTS + s, 1), :]).then_inc(adjT_loaded[s], 16)

        @block.gpsimd
        def _(pool):
            nc.gpsimd.memset(ones32[:, :], 1.0)
            nc.gpsimd.memset(ident32[:, :], 0.0).then_inc(consts_ready, 1)
            pool.wait_ge(consts_ready, 1)
            nc.gpsimd.affine_select(out=ident32[:, :], in_=ident32[:, :], compare_op=ALU.not_equal, fill=1.0,
                                    base=0, pattern=[[-1, P]], channel_multiplier=1).then_inc(consts_ready, 1)

            def unit(n, k, j, opening):
                pool.wait_ge(hshi_done, n + 1)
                nc.gpsimd.tensor_tensor(hs_lo[:, k % 2, :], h[:, bass.ds(j, 1), :].rearrange("p o d -> p (o d)"),
                                        hs_hi[:, k % 2, :].bitcast(fp32), ALU.subtract).then_inc(hslo_done, 1)
                if opening and k == 0:
                    return
                pool.wait_ge(e_done, n + 1)
                if opening and k == 1:
                    if not (isinstance(n, int) and n < TILES):
                        pool.wait_ge(z_done, pool_panel[0])
                    nc.gpsimd.tensor_tensor(esum[:, :], ework[:, 0, :], ework[:, 1, :], ALU.add).then_inc(esum_done, 2)
                else:
                    pool.wait_ge(esum_done, n)
                    nc.gpsimd.tensor_tensor(esum[:, :], esum[:, :], ework[:, k % 4, :], ALU.add).then_inc(esum_done, 1)

            pool_panel = [0]

            def body(b, c, opening=False):
                for k in range(BODY):
                    unit(b * BODY + k, k, c * BODY + k, opening)

            body(0, 0, True)
            with pool.Fori(1, BODIES) as c:
                body(c, c)
            with pool.Fori(1, PANELS) as panel:
                pool_panel[0] = panel
                body(panel * BODIES, 0, True)
                with pool.Fori(1, BODIES) as c:
                    body(panel * BODIES + c, c)

        @block.scalar
        def _(act):
            act.wait_ge(ab_copied, 1)
            nc.scalar.activation(gate_tmp[:, 0:1], ab[:, 0:1], ACT.Exp, scale=-1.0).then_inc(alpha_exp, 1)
            nc.scalar.mul(neg_half_beta[:, :], ab[:, 1:2], -0.5).then_inc(scalars_ready, 1)
            act.wait_ge(var_ready, 1)
            nc.scalar.activation(vb[:, :], va[:, :], ACT.Sqrt).then_inc(std_ready, 1)
            act.wait_ge(ln_ready, 1)
            for t in range(TILES):
                nc.scalar.activation(h[:, t, :], h[:, t, :], ACT.Relu, scale=rstd[:, t:t + 1],
                                     bias=shift[:, t:t + 1]).then_inc(h_ready, 1)
            act.wait_ge(ssq_ready, 1)
            nc.scalar.activation(vb[:, :], ssq[:, :], ACT.Sqrt).then_inc(norm_root, 1)
            act.wait_ge(rnorm_ready, 1)
            for g in range(GROUPS):
                if g >= 4:
                    act.wait_ge(u_split, g - 3)
                for t in range(PT):
                    last = nc.scalar.activation(ework[:, g % 4, t * P:(t + 1) * P], h[:, g * PT + t, :], ACT.Copy,
                                                scale=rnorm[:, g * PT + t:g * PT + t + 1])
                last.then_inc(u_ready, 1)

            def exps(n, kk, j, waits):
                if waits:
                    act.wait_ge(attn_done, n - 1)
                nc.scalar.activation(hs_hi[:, kk % 2, :], h[:, bass.ds(j, 1), :].rearrange("p o d -> p (o d)"),
                                     ACT.Copy).then_inc(hshi_done, 1)
                act.wait_ge(x_done, n + 1)
                nc.scalar.activation(e_hi[:, kk % 2, :], ework[:, kk % 4, :], ACT.Exp, bias=neg_half_beta[:, :],
                                     scale=ab[:, 1:2]).then_inc(ehi_done, 1)
                nc.scalar.activation(ework[:, kk % 4, :], ework[:, kk % 4, :], ACT.Exp, bias=neg_half_beta[:, :],
                                     scale=ab[:, 1:2]).then_inc(e_done, 1)

            def copy_attn(panel):
                act.wait_ge(attn_done, panel * TILES)
                nc.scalar.activation(attnT[:, bass.ds((panel - 1) * PW, PW)], attn_ps[:, :],
                                     ACT.Copy).then_inc(attn_copied, 1)

            def body(b, c, panel=None):
                for k in range(BODY):
                    if panel is not None and k == 2:
                        copy_attn(panel)
                    if not (is_first(b) and k == 0):
                        j = TILES - 1 if k == 0 and isinstance(c, int) else c * BODY + k - 1
                        exps(b * BODY + k - 1, (k - 1) % BODY, j, not (is_first(b) and k < 3))

            act.wait_ge(scalars_ready, 1)
            body(0, 0)
            with act.Fori(1, BODIES) as c:
                body(c, c)
            with act.Fori(1, PANELS) as panel:
                body(panel * BODIES, 0, panel)
                with act.Fori(1, BODIES) as c:
                    body(panel * BODIES + c, c)
            exps(UNITS - 1, BODY - 1, TILES - 1, True)
            copy_attn(PANELS)

            act.wait_ge(deg_ready, 1)
            nc.scalar.activation(vb[:, :], va[:, :], ACT.Sqrt).then_inc(deg_root, 1)
            act.wait_ge(dis_ready, 1)
            act.wait_ge(esum_done, UNITS)
            act.wait_ge(elo_done, UNITS)
            for g in range(GROUPS):
                if g >= 4:
                    act.wait_ge(dh_ready, g - 3)
                for t in range(PT):
                    last = nc.scalar.activation(ework[:, g % 4, t * P:(t + 1) * P], h[:, g * PT + t, :], ACT.Copy,
                                                scale=dis[:, g * PT + t:g * PT + t + 1])
                last.then_inc(dh_scaled, 1)
            for panel in range(PANELS):
                if panel >= 2:
                    act.wait_ge(out_stored[panel % 2], 16 * (panel // 2))
                    act.wait_ge(back_used, 2 * (panel - 1))
                else:
                    act.wait_ge(dh_ready, GROUPS)
                act.dma_start(ework[:, panel % 2, :].rearrange("p (t d) -> p t d", d=P),
                              x_t[:, panel * PT:(panel + 1) * PT, :]).then_inc(x_again[panel % 2], 16)
                act.wait_ge(diff_used, (panel + 1) * (TILES // LOAD))
                if panel >= 1:
                    act.wait_ge(back_done, 2 * panel)
                nc.scalar.activation(ework[:, 2, :], cos_ps[:, panel % 2, :], ACT.Copy).then_inc(diffT_copied, 1)
                act.wait_ge(out_ready, panel + 1)
                act.dma_start(out_t[:, panel * PT:(panel + 1) * PT, :],
                              ework[:, panel % 2, :].rearrange("p (t d) -> p t d", d=P)).then_inc(out_stored[panel % 2], 16)
            for s in range(2):
                act.wait_ge(out_stored[s], 16 * ((PANELS + 1 - s) // 2))

        @block.vector
        def _(dve):
            chain = [0]

            def link(ins):
                chain[0] += 1
                ins.then_inc(vec_chain, 1)
                dve.wait_ge(vec_chain, chain[0])

            def refine_root(value, root, tmp):
                link(nc.vector.reciprocal(tmp, root))
                link(nc.vector.tensor_tensor(tmp, tmp, value, ALU.mult))
                link(nc.vector.tensor_tensor(root, root, tmp, ALU.add))
                link(nc.vector.tensor_scalar(root, root, 0.5, None, ALU.mult))

            nc.vector.memset(onesb[:, :], 1.0)
            dve.wait_ge(consts_ready, 2)
            nc.vector.tensor_copy(ident16[:, :], ident32[:, :])
            nc.vector.tensor_copy(identb[:, :], ident32[:, :]).then_inc(idents_ready, 1)
            dve.wait_ge(ab_bcast, 1)
            nc.vector.tensor_copy(ab[:, :], ab_ps).then_inc(ab_copied, 1)
            dve.wait_ge(alpha_exp, 1)
            link(nc.vector.tensor_scalar(gate_tmp[:, 1:2], gate_tmp[:, 0:1], 1.0, None, ALU.add))
            link(nc.vector.reciprocal(gate[:, :], gate_tmp[:, 1:2]))
            link(nc.vector.tensor_scalar(neg_1_gate[:, :], gate[:, :], -1.0, -1.0, ALU.mult, ALU.add))

            for t in range(TILES):
                if t % (TILES // 2) == 0:
                    dve.wait_ge(x_loaded[t // (TILES // 2)], 16)
                last = nc.vector.bn_stats(out=stats[:, t, :], in_=h[:, t, :])
            link(last)
            for t in range(TILES):
                last = nc.vector.bn_aggr(out=mv[:, t, :], in_=stats[:, t, :])
            link(last)
            nc.vector.tensor_scalar(va[:, :], mv[:, :, 1], LN_EPS, None, ALU.add).then_inc(var_ready, 1)
            dve.wait_ge(std_ready, 1)
            refine_root(va[:, :], vb[:, :], vc[:, :])
            link(nc.vector.reciprocal(rstd[:, :], vb[:, :]))
            nc.vector.scalar_tensor_tensor(out=shift[:, :], in0=mv[:, :, 0], scalar=-1.0, in1=rstd[:, :],
                                           op0=ALU.mult, op1=ALU.mult).then_inc(ln_ready, 1)
            for t in range(TILES):
                dve.wait_ge(h_ready, t + 1)
                last = nc.vector.tensor_tensor_reduce(out=attnT[:, t * P:(t + 1) * P], in0=h[:, t, :], in1=h[:, t, :], scale=1.0,
                                                      scalar=0.0, op0=ALU.mult, op1=ALU.add,
                                                      accum_out=ssq[:, t:t + 1])
            link(last)
            nc.vector.tensor_scalar(ssq[:, :], ssq[:, :], COS_EPS * COS_EPS, None, ALU.max).then_inc(ssq_ready, 1)
            dve.wait_ge(norm_root, 1)
            refine_root(ssq[:, :], vb[:, :], vc[:, :])
            nc.vector.reciprocal(rnorm[:, :], vb[:, :]).then_inc(rnorm_ready, 1)
            for g in range(GROUPS + 1):
                if g < GROUPS:
                    hi, lo = rows16[g % 2]
                    dve.wait_ge(u_ready, g + 1)
                    if g >= 2:
                        dve.wait_ge(uT_done, 2 * (g - 1))
                    link(nc.vector.tensor_copy(hi, ework[:, g % 4, :]))
                    nc.vector.tensor_tensor(lo, ework[:, g % 4, :], hi, ALU.subtract).then_inc(u_split, 1)
                if g >= 1:
                    for part, dst in enumerate((uT_hi, uT_lo)):
                        dve.wait_ge(uT_done, 2 * (g - 1) + part + 1)
                        nc.vector.tensor_copy(dst[:, (g - 1) * PW:g * PW], uT_ps[part]).then_inc(uT_copied, 1)

            def evacuate(n, kk, stored):
                dve.wait_ge(transposed, n + 1)
                if kk % LOAD == 0 and stored is not None:
                    dve.wait_ge(adjT_stored[kk // LOAD], 16 * stored)
                nc.vector.tensor_copy(adjT[:, kk // LOAD, kk % LOAD, :], adjT_ps[:, :]).then_inc(adjT_ready, 1)

            def masked(n, kk, waits):
                dve.wait_ge(cos_done, n + 1)
                dve.wait_ge(adjT_ready, n + 1)
                if waits:
                    dve.wait_ge(esum_done, n - 3)
                nc.vector.tensor_tensor(ework[:, kk % 4, :], cos_ps[:, kk % 2, :], adjT[:, kk // LOAD, kk % LOAD, :],
                                        ALU.mult).then_inc(x_done, 1)

            def rest(n, kk):
                dve.wait_ge(e_done, n + 1)
                nc.vector.tensor_tensor(e_lo[:, kk % 2, :], ework[:, kk % 4, :], e_hi[:, kk % 2, :].bitcast(fp32),
                                        ALU.subtract).then_inc(elo_done, 1)

            def copy_deg(panel):
                dve.wait_ge(attn_done, panel * TILES)
                nc.vector.tensor_copy(deg[:, bass.ds((panel - 1) * PT, PT)], deg_ps).then_inc(deg_copied, 1)

            def copy_z(panel):
                dve.wait_ge(z_done, panel)
                nc.vector.tensor_copy(zsum[:, bass.ds((panel - 1) * PT, PT)], z_ps).then_inc(z_copied, 1)

            def body(b, panel=None, final=False):
                n0 = b * BODY
                for k in range(BODY):
                    if panel is not None and k == 2:
                        copy_deg(panel)
                    if panel is not None and k == 3:
                        copy_z(panel)
                    if not (final and k == BODY - 1):
                        if k < BODY - 1:
                            stored = None if is_first(b) else b
                        else:
                            stored = b + 1
                        evacuate(n0 + k + 1, (k + 1) % BODY, stored)
                    masked(n0 + k, k, not (is_first(b) and k < 4))
                    if not (is_first(b) and k == 0):
                        rest(n0 + k - 1, (k - 1) % BODY)

            evacuate(0, 0, None)
            body(0)
            with dve.Fori(1, BODIES) as c:
                body(c)
            with dve.Fori(1, PANELS - 1) as panel:
                body(panel * BODIES, panel)
                with dve.Fori(1, BODIES) as c:
                    body(panel * BODIES + c)
            body((PANELS - 1) * BODIES, PANELS - 1)
            if BODIES > 2:
                with dve.Fori(1, BODIES - 1) as c:
                    body((PANELS - 1) * BODIES + c)
            body(PANELS * BODIES - 1, None, True)
            rest(UNITS - 1, BODY - 1)
            copy_deg(PANELS)
            dve.wait_ge(deg_copied, PANELS)
            nc.vector.tensor_scalar(va[:, :], deg[:, :], 1.0, None, ALU.max).then_inc(deg_ready, 1)
            dve.wait_ge(deg_root, 1)
            refine_root(va[:, :], vb[:, :], vc[:, :])
            nc.vector.reciprocal(dis[:, :], vb[:, :]).then_inc(dis_ready, 1)
            for g in range(GROUPS):
                if g == 0:
                    dve.wait_ge(z_done, PANELS)
                dve.wait_ge(dh_scaled, g + 1)
                link(nc.vector.tensor_copy(dh_hi[:, g * PW:(g + 1) * PW], ework[:, g % 4, :]))
                nc.vector.tensor_tensor(dh_lo[:, g * PW:(g + 1) * PW], ework[:, g % 4, :],
                                        dh_hi[:, g * PW:(g + 1) * PW], ALU.subtract).then_inc(dh_ready, 1)
            copy_z(PANELS)
            dve.wait_ge(z_copied, PANELS)
            link(nc.vector.reciprocal(vc[:, :], zsum[:, :]))
            link(nc.vector.tensor_scalar(gz[:, :], vc[:, :], gate[:, 0:1], None, ALU.mult))
            for panel in range(PANELS):
                o = ework[:, panel % 2, :]
                hp = h[:, panel * PT:(panel + 1) * PT, :].rearrange("p t d -> p (t d)")
                dve.wait_ge(x_again[panel % 2], 16 * (panel // 2 + 1))
                link(nc.vector.scalar_tensor_tensor(out=o, in0=hp, scalar=neg_1_gate[:, 0:1], in1=o,
                                                    op0=ALU.mult, op1=ALU.add))
                for q in range(2):
                    dve.wait_ge(back_done, 2 * panel + q + 1)
                    for t in range(PT // 2):
                        i = q * (PT // 2) + t
                        row = panel * PT + i
                        oi = o[:, i * P:(i + 1) * P]
                        nc.vector.scalar_tensor_tensor(out=oi, in0=attn_ps[:, t * P:(t + 1) * P],
                                                       scalar=dis[:, row:row + 1], in1=oi,
                                                       op0=ALU.mult, op1=ALU.add)
                    link(nc.vector.memset(gate_tmp[:, 0:1], 0.0))
                    for t in range(PT // 2):
                        i = q * (PT // 2) + t
                        row = panel * PT + i
                        oi = o[:, i * P:(i + 1) * P]
                        last = nc.vector.scalar_tensor_tensor(out=oi, in0=attn_ps[:, HALF + t * P:HALF + (t + 1) * P],
                                                              scalar=gz[:, row:row + 1], in1=oi,
                                                              op0=ALU.mult, op1=ALU.add)
                    last.then_inc(back_used, 1)
                nc.vector.memset(gate_tmp[:, 1:2], 0.0).then_inc(out_ready, 1)

        @block.tensor
        def _(pe):
            pe.wait_ge(ab_loaded, 32)
            pe.wait_ge(idents_ready, 1)
            nc.tensor.matmul(ab_ps, ones32[0:1, :], ab_row[0:1, :], start=True, stop=True).then_inc(ab_bcast, 1)

            def transpose_unit(n, kk, loads):
                if kk % LOAD == 0:
                    pe.wait_ge(adj_loaded[kk // LOAD], 16 * loads)
                if not (isinstance(n, int) and n == 0):
                    pe.wait_ge(adjT_ready, n)
                for t in range(PT):
                    last = nc.tensor.transpose(adjT_ps[:, t * P:(t + 1) * P],
                                               adj_bf[:, kk // LOAD, t, (kk % LOAD) * P:(kk % LOAD + 1) * P, 1],
                                               identb[:, :])
                last.then_inc(transposed, 1)

            transpose_unit(0, 0, 1)
            for g in range(GROUPS):
                pe.wait_ge(u_split, g + 1)
                for part in range(2):
                    if g >= 1:
                        pe.wait_ge(uT_copied, 2 * (g - 1) + part + 1)
                    for t in range(PT):
                        last = nc.tensor.transpose(uT_ps[part][:, t * P:(t + 1) * P],
                                                   rows16[g % 2][part][:, t * P:(t + 1) * P], ident16[:, :])
                    last.then_inc(uT_done, 1)

            def cosines(n, kk, j, panel, waits):
                if waits:
                    pe.wait_ge(x_done, n - 1)
                uj_hi = uT_hi[:, bass.ds(j * P, P)]
                uj_lo = uT_lo[:, bass.ds(j * P, P)]
                for m, (s, src) in enumerate(((uj_hi, uT_hi), (uj_hi, uT_lo), (uj_lo, uT_hi))):
                    for q in range(2):
                        last = nc.tensor.matmul(cos_ps[:, kk % 2, q * HALF:(q + 1) * HALF], s,
                                                src[:, bass.ds(panel * PW + q * HALF, HALF)],
                                                start=(m == 0), stop=(m == 2), skip_group_check=True)
                last.then_inc(cos_done, 1)

            def sums(n, kk, first, final, panel_before=None):
                if panel_before is not None:
                    pe.wait_ge(deg_copied, panel_before)
                    pe.wait_ge(attn_copied, panel_before)
                for t in range(PT):
                    nc.tensor.matmul(deg_ps[:, t:t + 1], adjT[:, kk // LOAD, kk % LOAD, t * P:(t + 1) * P],
                                     onesb[:, :], start=(first and t == 0), stop=final, skip_group_check=True)
                pe.wait_ge(hslo_done, n + 1)
                pe.wait_ge(elo_done, n + 1)
                for m, (s, e) in enumerate(((hs_hi, e_hi), (hs_hi, e_lo), (hs_lo, e_hi))):
                    for q in range(2):
                        last = nc.tensor.matmul(attn_ps[:, q * HALF:(q + 1) * HALF], s[:, kk % 2, :],
                                                e[:, kk % 2, q * HALF:(q + 1) * HALF],
                                                start=(first and m == 0), stop=(final and m == 2),
                                                skip_group_check=True)
                last.then_inc(attn_done, 1)

            def z_sums(panel, start):
                pe.wait_ge(esum_done, panel * TILES)
                if panel_is_late(panel):
                    pe.wait_ge(z_copied, panel - 1)
                for t in range(PT):
                    last = nc.tensor.matmul(z_ps[:, t:t + 1], esum[:, t * P:(t + 1) * P], ones32[:, 0:1],
                                            start=(start and t == 0), stop=True, skip_group_check=True)
                last.then_inc(z_done, 1)

            def panel_is_late(panel):
                return isinstance(panel, int) and panel > 1

            def body(b, c, panel, opening=False, final=False):
                n0 = b * BODY
                late = opening and not is_first(b)
                for k in range(BODY):
                    if not (final and k == BODY - 1):
                        transpose_unit(n0 + k + 1, (k + 1) % BODY, b + 1 if k < BODY - 1 else b + 2)
                    cosines(n0 + k, k, c * BODY + k, panel, not (is_first(b) and k < 2))
                    if late and k == 3:
                        pe.wait_ge(z_copied, panel)
                    if not (is_first(b) and k < 2):
                        sums(n0 + k - 2, (k - 2) % BODY, opening and k == 2, opening and k == 1,
                             panel if late and k == 2 else None)
                    if late and k == 2:
                        z_sums(panel, False)

            pe.wait_ge(uT_copied, 2 * GROUPS)
            body(0, 0, 0, opening=True)
            with pe.Fori(1, BODIES) as c:
                body(c, c, 0)
            with pe.Fori(1, PANELS - 1) as panel:
                body(panel * BODIES, 0, panel, opening=True)
                with pe.Fori(1, BODIES) as c:
                    body(panel * BODIES + c, c, panel)
            body((PANELS - 1) * BODIES, 0, PANELS - 1, opening=True)
            if BODIES > 2:
                with pe.Fori(1, BODIES - 1) as c:
                    body((PANELS - 1) * BODIES + c, c, PANELS - 1)
            body(PANELS * BODIES - 1, BODIES - 1, PANELS - 1, final=True)
            sums(UNITS - 2, BODY - 2, False, False)
            sums(UNITS - 1, BODY - 1, False, True)
            pe.wait_ge(deg_copied, PANELS)
            z_sums(PANELS, True)

            CPP = TILES // LOAD

            def diffuse(chunk_in_panel, slot, parity, round_, first):
                pe.wait_ge(adjT_loaded[slot], 16 * round_)
                for k in range(LOAD):
                    for m, dh in enumerate((dh_hi, dh_lo)):
                        for q in range(2):
                            last = nc.tensor.matmul(cos_ps[:, parity, q * HALF:(q + 1) * HALF],
                                                    dh[:, bass.ds((chunk_in_panel * LOAD + k) * P, P)],
                                                    adjT_in[:, slot, k, q * HALF:(q + 1) * HALF],
                                                    start=(first and k == 0 and m == 0), stop=True,
                                                    skip_group_check=True)
                last.then_inc(diff_used, 1)

            def back(panel, q):
                pe.wait_ge(diffT_copied, panel + 1)
                if panel or q:
                    pe.wait_ge(back_used, 2 * panel + q)
                for t in range(PT // 2):
                    i = q * (PT // 2) + t
                    nc.tensor.transpose(attn_ps[:, t * P:(t + 1) * P], ework[:, 2, i * P:(i + 1) * P], ident32[:, :])
                    last = nc.tensor.transpose(attn_ps[:, HALF + t * P:HALF + (t + 1) * P],
                                               attnT[:, panel * PW + i * P:panel * PW + (i + 1) * P], ident32[:, :])
                last.then_inc(back_done, 1)

            RPP = CPP // LSLOTS
            pe.wait_ge(attn_copied, PANELS)
            for panel in range(PANELS):
                if panel >= 2:
                    pe.wait_ge(diffT_copied, panel - 1)
                for s in range(LSLOTS):
                    if panel == 0:
                        pe.wait_ge(dh_ready, s * LOAD // PT + 1)
                    diffuse(s, s, panel % 2, panel * RPP + 1, s == 0)
                    if s in (1, 2) and panel:
                        back(panel - 1, s - 1)
                if panel == 0:
                    pe.wait_ge(dh_ready, GROUPS)
                if RPP > 1:
                    with pe.Fori(1, RPP) as r:
                        for s in range(LSLOTS):
                            diffuse(r * LSLOTS + s, s, panel % 2, panel * RPP + r + 1, False)
            back(PANELS - 1, 0)
            back(PANELS - 1, 1)


def kernel(x, adj, L0_gnn_t, L0_gnn_alpha, L0_gnn_beta):
    import concourse.bacc as bacc
    from concourse.bass_utils import run_bass_kernel_spmd

    nc = bacc.Bacc("TRN2", target_bir_lowering=False, num_devices=1)
    arrays = {
        "x_in": np.ascontiguousarray(x),
        "adj_in_dram": np.ascontiguousarray(adj),
        "alpha_in": np.asarray(L0_gnn_alpha).reshape(1, 1),
        "beta_in": np.asarray(L0_gnn_beta).reshape(1, 1),
    }
    aps = [nc.dram_tensor(name, a.shape, mybir.dt.from_np(a.dtype), kind="ExternalInput").ap()
           for name, a in arrays.items()]
    out = nc.dram_tensor("out_dram", x.shape, mybir.dt.float32, kind="ExternalOutput").ap()
    gnn_block_kernel(nc, *aps, out)
    result = run_bass_kernel_spmd(nc, [arrays], core_ids=[0])
    return result.results[0]["out_dram"]
```
